# Optimizing a Trainium2 kernel written in Bass

```python
import numpy as np
import jax
import jax.numpy as jnp

def _softmax(x, axis=-1):
    return jax.nn.softmax(x, axis=axis)

def _gelu(x):
    return jax.nn.gelu(x, approximate=True)

def _silu(x):
    return jax.nn.silu(x)

def _sigmoid(x):
    return jax.nn.sigmoid(x)

def _layernorm(x, axis=-1, eps=1e-05):
    m = jnp.mean(x, axis=axis, keepdims=True)
    v = jnp.var(x, axis=axis, keepdims=True)
    return (x - m) / jnp.sqrt(v + eps)

def _scatter_add(tgt, idx, src, axis=0):
    return tgt.at[idx].add(src)

def _segment_sum(src, seg, n):
    return jax.ops.segment_sum(src, seg, n)
kernel_name = 'mk_cond_resid_d1_seqx_r2_b7dd5e'

def setup_inputs(seed: int=0):
    np.random.seed(seed)
    _w = jnp.asarray

    def _rec_inputs():
        import jax
        import jax.numpy as jnp
        _rk = jax.random.key(seed)
        x = -0.000125 + 0.9999 * jax.random.normal(jax.random.fold_in(_rk, 1), (32, 128, 2048), jnp.float32)
        _lenS = 128 - jax.random.randint(jax.random.fold_in(_rk, 7), (32,), 0, max(1, 128 // 4) + 1, jnp.int32)
        _lenS2 = 128 - jax.random.randint(jax.random.fold_in(_rk, 8), (32,), 0, max(1, 128 // 4) + 1, jnp.int32)
        itok_B_6_15 = jax.random.randint(jax.random.fold_in(_rk, 11), (32,), 6, 16, jnp.int32)
        return (x, itok_B_6_15)
    x, itok_B_6_15 = _rec_inputs()

    def _L0_cond_setup():
        import jax, jax.numpy as jnp
        import numpy as np
        B, S, D_IN, D_OUT = (4, 1024, 2048, 2048)
        RANK, MAX_LORAS = (16, 32)
        key = jax.random.key(seed)
        ks = jax.random.split(key, 6)
        x = jax.random.normal(ks[0], (B, S, D_IN), dtype=jnp.float32)
        adapter_ids = jax.random.randint(ks[1], (B,), 0, MAX_LORAS)
        base_weight = jax.random.normal(ks[2], (D_OUT, D_IN), dtype=jnp.float32) * D_IN ** (-0.5)
        base_bias = jax.random.normal(ks[3], (D_OUT,), dtype=jnp.float32) * 0.01
        lora_A_w = jax.random.normal(ks[4], (MAX_LORAS, RANK, D_IN), dtype=jnp.float32) * D_IN ** (-0.5)
        lora_B_w = jax.random.normal(ks[5], (MAX_LORAS, D_OUT, RANK), dtype=jnp.float32) * RANK ** (-0.5)
        return {'x': x, 'adapter_ids': adapter_ids, 'base_weight': base_weight, 'base_bias': base_bias, 'lora_A_w': lora_A_w, 'lora_B_w': lora_B_w}
    _L0_cond_all = _L0_cond_setup()
    _L0_cond_in = {k: v for k, v in _L0_cond_all.items() if k in ('base_weight', 'base_bias', 'lora_A_w', 'lora_B_w')}
    del _L0_cond_all
    return {'x': x, 'itok_B_6_15': itok_B_6_15, 'L0_cond_base_weight': _L0_cond_in['base_weight'], 'L0_cond_base_bias': _L0_cond_in['base_bias'], 'L0_cond_lora_A_w': _L0_cond_in['lora_A_w'], 'L0_cond_lora_B_w': _L0_cond_in['lora_B_w']}

def reference(x, itok_B_6_15, L0_cond_base_weight, L0_cond_base_bias, L0_cond_lora_A_w, L0_cond_lora_B_w):
    import jax
    import jax.numpy as jnp

    def _L0_cond_ref(x, adapter_ids, base_weight, base_bias, lora_A_w, lora_B_w):
        import jax, jax.numpy as jnp
        import numpy as np
        B, S, D_IN, D_OUT = (4, 1024, 2048, 2048)
        RANK, MAX_LORAS = (16, 32)
        result = jnp.einsum('bsd,od->bso', x, base_weight) + base_bias
        A = lora_A_w[adapter_ids]
        Bw = lora_B_w[adapter_ids]
        h = jnp.einsum('bsd,brd->bsr', x, A)
        lora_out = jnp.einsum('bsr,bor->bso', h, Bw)
        result = result + lora_out
        return result.astype(x.dtype)
    x = x + _L0_cond_ref(x, itok_B_6_15, L0_cond_base_weight, L0_cond_base_bias, L0_cond_lora_A_w, L0_cond_lora_B_w)
    return x

_drawn_inputs = setup_inputs


def setup_inputs(seed=0):
    import zlib

    import numpy as np

    out = dict(_drawn_inputs(seed))
    spreads = {}
    factors = {'L0_cond_base_bias': 8.0}
    for name, (base, spread) in spreads.items():
        noise = np.random.default_rng([zlib.crc32(name.encode()), seed]).standard_normal(out[name].shape)
        drawn = base * np.exp(spread * noise) if base else spread * noise
        out[name] = jnp.asarray(drawn.astype(out[name].dtype))
    for name, factor in factors.items():
        out[name] = (out[name] * factor).astype(out[name].dtype)
    return out
```

```python
from contextlib import ExitStack

import numpy as np
import concourse.bass as bass
from concourse import mybir
from concourse.alu_op_type import AluOpType as ALU

P = 128
SEQS = 32
ROWS = 128
D_IN = 2048
D_OUT = 2048
RANK = 16
ADAPTERS = 32
CHUNKS = D_IN // P
GROUPS = 4
GC = CHUNKS // GROUPS
SWEEPS = 2
HALF = D_OUT // SWEEPS
BANK = 512
BANKS = HALF // BANK
PAIRS = SEQS // 2
AR = 2 * RANK
COPIES = P // RANK
DMA = 16


def lora_kernel(nc, xT, x, wT, bias, aT, bT, ids, out):
    f32, f32r = mybir.dt.float32, mybir.dt.float32r
    COPY = mybir.ActivationFunctionType.Copy
    ctx = ExitStack()
    with ctx:
        slab_at = (nc.sbuf_base + 31) // 32 * 32
        SLAB = 204 * 1024
        ctx.enter_context(nc.sbuf_tensor("slab", [P, SLAB], mybir.dt.uint8))
        place = [slab_at]

        def at(name, shape, dt, offset=None):
            o = place[0] if offset is None else offset
            if offset is None:
                place[0] += 4 * int(np.prod(shape[1:]))
                assert place[0] <= slab_at + SLAB
            return nc.alloc_sbuf_tensor_at(name, shape, dt, offset=o)

        w_hi = at("w_hi", [P, CHUNKS, HALF], f32r)
        w_raw_at = place[0]
        w_lo = at("w_lo", [P, CHUNKS, HALF], f32r)
        w_raw = at("w_raw", [P, CHUNKS, HALF], f32, offset=w_raw_at)
        x_hi = at("x_hi", [P, CHUNKS, ROWS], f32r)
        x_raw_at = place[0]
        x_lo = at("x_lo", [P, 2, CHUNKS, ROWS], f32r)
        x_raw = at("x_raw", [P, 2, CHUNKS, ROWS], f32, offset=x_raw_at)
        res = at("res", [P, 2, HALF], f32)
        bias_sb = at("bias_sb", [P, D_OUT], f32)
        a_raw = at("a_raw", [P, CHUNKS, RANK], f32)
        a_split = at("a_split", [P, 2, CHUNKS, AR], f32r)
        b_raw = at("b_raw", [P, HALF], f32)
        b_stack = at("b_stack", [P, 2, HALF], f32r)
        h_stack = at("h_stack", [P, 2, ROWS], f32r)
        h_keep = at("h_keep", [P, SEQS * ROWS], f32r)
        ids_sb = at("ids_sb", [1, SEQS], mybir.dt.int32)

        acc = [ctx.enter_context(nc.psum_tensor(f"acc{j}", [P, BANKS, BANK], f32)) for j in range(2)]
        h_ps = [ctx.enter_context(nc.psum_tensor(f"h_ps{j}", [P, BANK], f32)) for j in range(2)]

        def sem(name):
            return ctx.enter_context(nc.semaphore(name))

        ids_in = sem("ids_in")
        bias_in = sem("bias_in")
        x_in = [sem(f"x_in{j}") for j in range(2)]
        res_in = [sem(f"res_in{j}") for j in range(2)]
        a_in = sem("a_in")
        b_in = sem("b_in")
        w_in = [sem(f"w_in{k}") for k in range(CHUNKS)]
        stored = [sem(f"stored{j}") for j in range(2)]
        x_hi_done = sem("x_hi_done")
        x_split = sem("x_split")
        w_hi_done = sem("w_hi_done")
        w_split = sem("w_split")
        a_hi_done = sem("a_hi_done")
        a_ready = sem("a_ready")
        b_hi_done = sem("b_hi_done")
        b_ready = sem("b_ready")
        group_used = sem("group_used")
        h_done = sem("h_done")
        h_hi_done = sem("h_hi_done")
        h_ready = sem("h_ready")
        h_kept = sem("h_kept")
        h_back = sem("h_back")
        acc_done = sem("acc_done")
        acc_read = sem("acc_read")
        res_biased = sem("res_biased")

        block = ctx.enter_context(nc.Block())

        @block.sync
        def _(sp):
            def load_x(step, j, seq):
                sp.dma_start(x_raw[:, j], xT[seq]).then_inc(x_in[j], DMA)

            def load_res(seq, j, half):
                sp.dma_start(res[:, j], x[seq, :, half * HALF:(half + 1) * HALF]).then_inc(res_in[j], DMA)

            def adapter_of(seq):
                return sp.value_load(ids_sb[0:1, bass.ds(seq, 1)], min_val=0, max_val=ADAPTERS - 1)

            def load_a(adapter):
                sp.dma_start(a_raw[:], aT[bass.ds(adapter, 1)]).then_inc(a_in, DMA)

            def load_b(adapter, half):
                rows = bT[bass.ds(adapter, 1), :, half * HALF:(half + 1) * HALF]
                sp.dma_start(b_raw[:], rows.to_broadcast([COPIES, RANK, HALF])).then_inc(b_in, DMA)

            def load_w(k, half):
                sp.dma_start(w_raw[:, k], wT[half, k]).then_inc(w_in[k], DMA)

            sp.dma_start(ids_sb[:], ids).then_inc(ids_in, DMA)
            load_x(0, 0, 0)
            load_w(0, 0)
            sp.wait_ge(ids_in, DMA)
            adapter = adapter_of(0)
            load_a(adapter)
            load_b(adapter, 0)
            for k in range(1, CHUNKS):
                load_w(k, 0)
            sp.dma_start(bias_sb[:], bias.to_broadcast([P, D_OUT])).then_inc(bias_in, DMA)
            load_x(1, 1, 1)
            load_res(0, 0, 0)
            load_res(1, 1, 0)

            def step(i, j, sweep, last):
                seq = 2 * i + j
                t = sweep * SEQS + seq
                n = sweep * PAIRS + i
                wraps = last and j == 1
                if not (sweep == 1 and wraps):
                    adapter = adapter_of(0 if wraps else seq + 1)
                if sweep == 0:
                    if not wraps:
                        sp.wait_ge(a_hi_done, t + 1)
                        sp.wait_ge(a_ready, t + 1)
                        load_a(adapter)
                if not (sweep == 1 and wraps):
                    sp.wait_ge(b_ready, t + 1)
                    load_b(adapter, 1 if wraps else sweep)
                if sweep == 0 and wraps:
                    for g in range(GROUPS):
                        sp.wait_ge(group_used, GROUPS * t + g + 1)
                        for k in range(g * GC, (g + 1) * GC):
                            load_w(k, 1)
                if not (sweep == 1 and last):
                    sp.wait_ge(group_used, GROUPS * (t + 1))
                    load_x(t + 2, j, j if last else seq + 2)
                sp.wait_ge(acc_read, t + 1)
                sp.dma_start(out[seq, :, sweep * HALF:(sweep + 1) * HALF], res[:, j]).then_inc(stored[j], DMA)
                if not (sweep == 1 and last):
                    sp.wait_ge(stored[j], DMA * (n + 1))
                    load_res(j if last else seq + 2, j, 1 if last else sweep)

            for sweep in range(SWEEPS):
                with sp.Fori(0, PAIRS - 1) as i:
                    for j in range(2):
                        step(i, j, sweep, False)
                for j in range(2):
                    step(PAIRS - 1, j, sweep, True)
            for j in range(2):
                sp.wait_ge(stored[j], DMA * SWEEPS * PAIRS)

        @block.scalar
        def _(act):
            def x_high(g, t, j, n, first):
                if g == 0:
                    act.wait_ge(x_in[j], DMA * (n + 1))
                if not first:
                    act.wait_ge(group_used, GROUPS * (t - 1) + g + 1)
                s = slice(g * GC, (g + 1) * GC)
                nc.scalar.activation(x_hi[:, s], x_raw[:, j, s], COPY).then_inc(x_hi_done, 1)

            def w_high(k, sweep):
                act.wait_ge(w_in[k], DMA * (sweep + 1))
                nc.scalar.activation(w_hi[:, k], w_raw[:, k], COPY).then_inc(w_hi_done, 1)

            def a_high(t, j, first):
                act.wait_ge(a_in, DMA * (t + 1))
                if not first:
                    act.wait_ge(group_used, GROUPS * (t - 1))
                nc.scalar.activation(a_split[:, j, :, 0:RANK], a_raw[:], COPY).then_inc(a_hi_done, 1)

            def b_high(t, j, first):
                act.wait_ge(b_in, DMA * (t + 1))
                if not first:
                    act.wait_ge(acc_done, t - 1)
                nc.scalar.activation(b_stack[:, j], b_raw[:], COPY).then_inc(b_hi_done, 1)

            def h_high(t, j):
                act.wait_ge(h_done, t + 1)
                nc.scalar.activation(h_stack[0:AR, j], h_ps[j][0:AR, 0:ROWS], COPY)
                nc.scalar.activation(h_stack[64:64 + AR, j], h_ps[j][0:AR, 0:ROWS], COPY).then_inc(h_hi_done, 1)

            def step(i, j, sweep, first, last):
                t = sweep * SEQS + 2 * i + j
                n = sweep * PAIRS + i
                more = not (sweep == 1 and last and j == 1)
                if more:
                    jn, nn = 1 - j, n + j
                    very_first = first and j == 0
                    if sweep == 0 and not (last and j == 1):
                        a_high(t + 1, jn, very_first)
                    b_high(t + 1, jn, very_first)
                    for g in range(GROUPS - 1):
                        x_high(g, t + 1, jn, nn, False)
                if sweep == 0:
                    h_high_guarded(t, j, first)
                if more:
                    x_high(GROUPS - 1, t + 1, jn, nn, False)

            def h_high_guarded(t, j, first):
                if not first:
                    act.wait_ge(acc_done, t - 1)
                    act.wait_ge(h_kept, t - 1)
                h_high(t, j)

            x_high(0, 0, 0, 0, True)
            a_high(0, 0, True)
            for k in range(CHUNKS):
                w_high(k, 0)
                if k % GC == 1 and k // GC + 1 < GROUPS:
                    x_high(k // GC + 1, 0, 0, 0, True)
                if k == GC:
                    b_high(0, 0, True)
            for j in range(2):
                step(0, j, 0, True, False)
            with act.Fori(1, PAIRS - 1) as i:
                for j in range(2):
                    step(i, j, 0, False, False)
            for j in range(2):
                step(PAIRS - 1, j, 0, False, True)
            for k in range(CHUNKS):
                w_high(k, 1)
            with act.Fori(0, PAIRS - 1) as i:
                for j in range(2):
                    step(i, j, 1, False, False)
            for j in range(2):
                step(PAIRS - 1, j, 1, False, True)

        @block.vector
        def _(dve):
            def x_low(g, t, j):
                dve.wait_ge(x_hi_done, GROUPS * t + g + 1)
                s = slice(g * GC, (g + 1) * GC)
                nc.vector.tensor_tensor(x_lo[:, j, s], x_raw[:, j, s], x_hi[:, s], ALU.subtract).then_inc(x_split, 1)

            def w_low(k, sweep):
                dve.wait_ge(w_hi_done, sweep * CHUNKS + k + 1)
                nc.vector.tensor_tensor(w_lo[:, k], w_raw[:, k], w_hi[:, k], ALU.subtract).then_inc(w_split, 1)

            def a_low(t, j):
                dve.wait_ge(a_hi_done, t + 1)
                nc.vector.tensor_tensor(a_split[:, j, :, RANK:AR], a_raw[:], a_split[:, j, :, 0:RANK],
                                        ALU.subtract).then_inc(a_ready, 1)

            def b_low(t, j):
                dve.wait_ge(b_hi_done, t + 1)
                nc.vector.tensor_tensor(b_stack[64:P, j], b_raw[64:P], b_stack[64:P, j],
                                        ALU.subtract).then_inc(b_ready, 1)

            def h_low(t, j):
                dve.wait_ge(h_hi_done, t + 1)
                nc.vector.tensor_tensor(h_stack[32:32 + AR, j], h_ps[j][0:AR, 0:ROWS], h_stack[0:AR, j],
                                        ALU.subtract)
                nc.vector.tensor_tensor(h_stack[96:96 + AR, j], h_ps[j][0:AR, 0:ROWS], h_stack[0:AR, j],
                                        ALU.subtract).then_inc(h_ready, 1)

            def finish(t, j):
                dve.wait_ge(res_biased, t + 1)
                dve.wait_ge(acc_done, t + 1)
                for o in range(BANKS):
                    s = slice(o * BANK, (o + 1) * BANK)
                    last = nc.vector.tensor_tensor(res[:, j, s], acc[j][:, o], res[:, j, s], ALU.add)
                last.then_inc(acc_read, 1)

            def step(i, j, sweep, last):
                t = sweep * SEQS + 2 * i + j
                more = not (sweep == 1 and last and j == 1)
                if more:
                    if sweep == 0 and not (last and j == 1):
                        a_low(t + 1, 1 - j)
                    b_low(t + 1, 1 - j)
                    for g in range(GROUPS - 1):
                        x_low(g, t + 1, 1 - j)
                if sweep == 0:
                    h_low(t, j)
                finish(t, j)
                if more:
                    x_low(GROUPS - 1, t + 1, 1 - j)

            x_low(0, 0, 0)
            a_low(0, 0)
            for k in range(CHUNKS):
                w_low(k, 0)
                if k % GC == 1 and k // GC + 1 < GROUPS:
                    x_low(k // GC + 1, 0, 0)
                if k == GC:
                    b_low(0, 0)
            with dve.Fori(0, PAIRS - 1) as i:
                for j in range(2):
                    step(i, j, 0, False)
            for j in range(2):
                step(PAIRS - 1, j, 0, True)
            for k in range(CHUNKS):
                w_low(k, 1)
            with dve.Fori(0, PAIRS - 1) as i:
                for j in range(2):
                    step(i, j, 1, False)
            for j in range(2):
                step(PAIRS - 1, j, 1, True)

        @block.gpsimd
        def _(pool):
            pool.wait_ge(bias_in, DMA)

            def step(i, j, sweep, first):
                seq = 2 * i + j
                t = sweep * SEQS + seq
                n = sweep * PAIRS + i
                if sweep == 1:
                    pool.wait_ge(acc_done, t - 1)
                    nc.gpsimd.tensor_copy(h_stack[:, j], h_keep[:, bass.ds(seq * ROWS, ROWS)]).then_inc(h_back, 1)
                pool.wait_ge(res_in[j], DMA * (n + 1))
                s = slice(sweep * HALF, (sweep + 1) * HALF)
                nc.gpsimd.tensor_tensor(res[:, j], res[:, j], bias_sb[:, s], ALU.add).then_inc(res_biased, 1)
                if sweep == 0:
                    pool.wait_ge(h_ready, t + 1)
                    nc.gpsimd.tensor_copy(h_keep[:, bass.ds(seq * ROWS, ROWS)], h_stack[:, j]).then_inc(h_kept, 1)

            with pool.Fori(0, PAIRS) as i:
                for j in range(2):
                    step(i, j, 0, False)
            pool.wait_ge(h_kept, SEQS)
            with pool.Fori(0, PAIRS) as i:
                for j in range(2):
                    step(i, j, 1, False)

        @block.tensor
        def _(pe):
            def project_down(g, j):
                for k in range(g * GC, (g + 1) * GC):
                    nc.tensor.matmul(h_ps[j][0:AR, 0:ROWS], a_split[:, j, k], x_hi[:, k],
                                     start=(k == 0), stop=False)
                    mm = nc.tensor.matmul(h_ps[j][0:AR, 0:ROWS], a_split[:, j, k], x_lo[:, j, k],
                                          start=False, stop=(k == CHUNKS - 1))
                if g == GROUPS - 1:
                    mm.then_inc(h_done, 1)

            def base_products(k, j):
                for n, (xs, ws) in enumerate(((x_hi[:, k], w_hi), (x_hi[:, k], w_lo), (x_lo[:, j, k], w_hi))):
                    for o in range(BANKS):
                        mm = nc.tensor.matmul(acc[j][:, o], xs, ws[:, k, o * BANK:(o + 1) * BANK],
                                              start=(k == 0 and n == 0), stop=False)
                return mm

            def step(i, j, sweep, first):
                t = sweep * SEQS + 2 * i + j
                if not first:
                    pe.wait_ge(acc_read, t - 1)
                    if sweep == 0:
                        pe.wait_ge(h_ready, t - 1)
                for g in range(GROUPS):
                    pe.wait_ge(x_split, GROUPS * t + g + 1)
                    if sweep == 0:
                        if g == 0:
                            pe.wait_ge(a_ready, t + 1)
                        project_down(g, j)
                    for k in range(g * GC, (g + 1) * GC):
                        pe.wait_ge(w_split, sweep * CHUNKS + k + 1)
                        mm = base_products(k, j)
                    mm.then_inc(group_used, 1)
                pe.wait_ge(b_ready, t + 1)
                if sweep == 0:
                    pe.wait_ge(h_ready, t + 1)
                else:
                    pe.wait_ge(h_back, t - SEQS + 1)
                for o in range(BANKS):
                    mm = nc.tensor.matmul(acc[j][:, o], h_stack[:, j], b_stack[:, j, o * BANK:(o + 1) * BANK],
                                          start=False, stop=True)
                mm.then_inc(acc_done, 1)

            for j in range(2):
                step(0, j, 0, True)
            with pe.Fori(1, PAIRS) as i:
                for j in range(2):
                    step(i, j, 0, False)
            with pe.Fori(0, PAIRS) as i:
                for j in range(2):
                    step(i, j, 1, False)


def kernel(x, itok_B_6_15, L0_cond_base_weight, L0_cond_base_bias, L0_cond_lora_A_w, L0_cond_lora_B_w):
    import concourse.bacc as bacc
    from concourse.bass_utils import run_bass_kernel_spmd

    def laid(a):
        return np.ascontiguousarray(a)

    x = np.asarray(x)
    w = np.asarray(L0_cond_base_weight)
    a = np.asarray(L0_cond_lora_A_w)
    b = np.asarray(L0_cond_lora_B_w)
    arrays = {
        "xT": laid(x.reshape(SEQS, ROWS, CHUNKS, P).transpose(0, 3, 2, 1)),
        "x": laid(x),
        "wT": laid(w.reshape(SWEEPS, HALF, CHUNKS, P).transpose(0, 2, 3, 1)),
        "bias": laid(np.asarray(L0_cond_base_bias).reshape(1, D_OUT)),
        "aT": laid(a.reshape(ADAPTERS, RANK, CHUNKS, P).transpose(0, 3, 2, 1)),
        "bT": laid(b.transpose(0, 2, 1)),
        "ids": laid(np.asarray(itok_B_6_15).reshape(1, SEQS)),
    }
    nc = bacc.Bacc("TRN2", target_bir_lowering=False, num_devices=1)
    aps = [nc.dram_tensor(name, v.shape, mybir.dt.from_np(v.dtype), kind="ExternalInput").ap()
           for name, v in arrays.items()]
    out = nc.dram_tensor("out", (SEQS, ROWS, D_OUT), mybir.dt.float32, kind="ExternalOutput").ap()
    lora_kernel(nc, *aps, out)
    r = run_bass_kernel_spmd(nc, [arrays], core_ids=[0])
    return r.results[0]["out"]
```

```python
from contextlib import ExitStack

import numpy as np
import concourse.bass as bass
from concourse import mybir
from concourse.alu_op_type import AluOpType as ALU

P = 128
SEQS = 32
ROWS = 128
D_IN = 2048
D_OUT = 2048
RANK = 16
ADAPTERS = 32
CHUNKS = D_IN // P
GROUPS = 4
GC = CHUNKS // GROUPS
SWEEPS = 2
HALF = D_OUT // SWEEPS
BANK = 512
PAIRS = SEQS // 2
AC = 2 * RANK
W_AT = AC
A_AT = (0, W_AT + HALF)
WIDE = W_AT + HALF + AC
BANKS_A = 3
COLS_A = (HALF + AC) // BANKS_A
BANKS_W = HALF // BANK
B_COPIES = P // 2 // RANK
DMA = 16


def pieces(sweep, j):
    if sweep == 1:
        return [(o, 0, BANK, o * BANK) for o in range(BANKS_W)]
    found, out = [], 0
    for o in range(BANKS_A):
        low = AC if (j == 0 and o == 0) else 0
        n = COLS_A - AC if o == (0, BANKS_A - 1)[j] else COLS_A
        found.append((o, low, n, out))
        out += n
    return found


H_BANK = (0, BANKS_A - 1)
H_AT = (0, COLS_A - AC)


def lora_kernel(nc, xT, x, wT, bias, aT, bT, ids, out):
    f32, f32r = mybir.dt.float32, mybir.dt.float32r
    COPY = mybir.ActivationFunctionType.Copy
    ctx = ExitStack()
    with ctx:
        slab_at = (nc.sbuf_base + 31) // 32 * 32
        SLAB = 207 * 1024
        ctx.enter_context(nc.sbuf_tensor("slab", [P, SLAB], mybir.dt.uint8))
        place = [slab_at]

        def at(name, shape, dt, offset=None):
            o = place[0] if offset is None else offset
            if offset is None:
                place[0] += 4 * int(np.prod(shape[1:]))
                assert place[0] <= slab_at + SLAB
            return nc.alloc_sbuf_tensor_at(name, shape, dt, offset=o)

        w_hi = at("w_hi", [P, CHUNKS, WIDE], f32r)
        w_raw_at = place[0]
        w_lo = at("w_lo", [P, CHUNKS, HALF], f32r)
        w_raw = at("w_raw", [P, CHUNKS, HALF], f32, offset=w_raw_at)
        x_hi = at("x_hi", [P, GROUPS, GC, ROWS], f32r)
        x_raw_at = place[0]
        x_lo = at("x_lo", [P, 2, CHUNKS, ROWS], f32r)
        x_raw = at("x_raw", [P, 2, CHUNKS, ROWS], f32, offset=x_raw_at)
        res = at("res", [P, 2, HALF], f32)
        bias_sb = at("bias_sb", [P, D_OUT], f32)
        a_raw = at("a_raw", [P, CHUNKS, RANK], f32)
        b_raw = at("b_raw", [P // 2, HALF], f32)
        b_stack = at("b_stack", [P, 2, HALF], f32r)
        h_cols = at("h_cols", [P, 2, 2, 2, AC], f32r)
        h_stack = at("h_stack", [P, 2, ROWS], f32r)
        h_keep = at("h_keep", [P, SEQS * ROWS], f32r)
        eye_raw = at("eye_raw", [P, P], f32)
        eye = at("eye", [P, P], f32r)
        ids_sb = at("ids_sb", [1, SEQS], mybir.dt.int32)

        acc = [ctx.enter_context(nc.psum_tensor(f"acc{j}", [P, BANKS_A, BANK], f32)) for j in range(2)]
        turned = ctx.enter_context(nc.psum_tensor("turned", [P, BANK], f32))

        def sem(name):
            return ctx.enter_context(nc.semaphore(name))

        ids_in = sem("ids_in")
        bias_in = sem("bias_in")
        x_first = [[sem(f"x_first{j}_{g}") for g in range(GROUPS)] for j in range(2)]
        x_in = [sem(f"x_in{j}") for j in range(2)]
        res_in = [sem(f"res_in{j}") for j in range(2)]
        a_in = sem("a_in")
        b_in = sem("b_in")
        w_in = [sem(f"w_in{k}") for k in range(CHUNKS)]
        stored = [sem(f"stored{j}") for j in range(2)]
        eye_filled = sem("eye_filled")
        eye_ready = sem("eye_ready")
        x_hi_done = sem("x_hi_done")
        x_split = sem("x_split")
        w_hi_done = sem("w_hi_done")
        w_split = sem("w_split")
        a_hi_done = sem("a_hi_done")
        a_ready = sem("a_ready")
        b_hi_done = sem("b_hi_done")
        b_ready = sem("b_ready")
        group_used = sem("group_used")
        h_done = sem("h_done")
        h_hi_done = sem("h_hi_done")
        h_cols_ready = sem("h_cols_ready")
        h_turned = sem("h_turned")
        h_ready = sem("h_ready")
        h_kept = sem("h_kept")
        h_back = sem("h_back")
        acc_done = sem("acc_done")
        acc_read = sem("acc_read")
        res_biased = sem("res_biased")

        block = ctx.enter_context(nc.Block())

        def turn(t, g):
            if isinstance(t, int) and t < 2:
                return 2 * g + t
            return GROUPS * t + g

        def slot(t, g):
            return (2 * g + t) % GROUPS if isinstance(t, int) and t < 2 else g

        @block.sync
        def _(sp):
            def load_x(j, seq):
                sp.dma_start(x_raw[:, j], xT[seq]).then_inc(x_in[j], DMA)

            def load_x_group(j, seq, g, landed):
                s = slice(g * GC, (g + 1) * GC)
                sp.dma_start(x_raw[:, j, s], xT[seq, :, s]).then_inc(landed, DMA)

            def load_res(seq, j, half):
                sp.dma_start(res[:, j], x[seq, :, half * HALF:(half + 1) * HALF]).then_inc(res_in[j], DMA)

            def adapter_of(seq):
                return sp.value_load(ids_sb[0:1, bass.ds(seq, 1)], min_val=0, max_val=ADAPTERS - 1)

            def load_a(adapter):
                sp.dma_start(a_raw[:], aT[bass.ds(adapter, 1)]).then_inc(a_in, DMA)

            def load_b(adapter, half):
                rows = bT[bass.ds(adapter, 1), :, half * HALF:(half + 1) * HALF]
                sp.dma_start(b_raw[:], rows.to_broadcast([B_COPIES, RANK, HALF])).then_inc(b_in, DMA)

            def load_w(k, half):
                sp.dma_start(w_raw[:, k], wT[half, k]).then_inc(w_in[k], DMA)

            def store(seq, j, half):
                sp.dma_start(out[seq, :, half * HALF:(half + 1) * HALF], res[:, j]).then_inc(stored[j], DMA)

            sp.dma_start(ids_sb[:], ids).then_inc(ids_in, DMA)
            load_x_group(0, 0, 0, x_first[0][0])
            load_w(0, 0)
            sp.wait_ge(ids_in, DMA)
            adapter = adapter_of(0)
            load_a(adapter)
            load_x_group(1, 1, 0, x_first[1][0])
            for k in range(1, GC):
                load_w(k, 0)
            load_b(adapter, 0)
            for j in range(2):
                load_x_group(j, j, 1, x_first[j][1])
            adapter = adapter_of(1)
            sp.wait_ge(a_ready, 1)
            load_a(adapter)
            for g in range(1, GROUPS):
                for k in range(g * GC, (g + 1) * GC):
                    load_w(k, 0)
                if g + 1 < GROUPS:
                    for j in range(2):
                        load_x_group(j, j, g + 1, x_first[j][g + 1])
            sp.wait_ge(b_ready, 1)
            load_b(adapter, 0)
            sp.dma_start(bias_sb[:], bias.to_broadcast([P, D_OUT])).then_inc(bias_in, DMA)
            load_res(0, 0, 0)
            load_res(1, 1, 0)
            adapter = adapter_of(2)
            sp.wait_ge(a_ready, 2)
            load_a(adapter)
            for g in range(GROUPS):
                for j in range(2):
                    if g < GROUPS - 1:
                        sp.wait_ge(group_used, turn(j, g) + 1)
                    else:
                        sp.wait_ge(h_done, j + 1)
                    load_x_group(j, j + 2, g, x_in[j])
            sp.wait_ge(b_ready, 2)
            load_b(adapter, 0)
            for j in range(2):
                sp.wait_ge(acc_read, j + 1)
                store(j, j, 0)
                sp.wait_ge(stored[j], DMA)
                load_res(j + 2, j, 0)

            def step(i, j, sweep, last):
                seq = 2 * i + j
                t = sweep * SEQS + seq
                n = sweep * PAIRS + i
                wraps = last and j == 1
                if not (sweep == 1 and wraps):
                    adapter = adapter_of(0 if wraps else seq + 1)
                if sweep == 0 and not wraps:
                    sp.wait_ge(a_ready, t + 1)
                    load_a(adapter)
                if not (sweep == 1 and wraps):
                    sp.wait_ge(b_ready, t + 1)
                    load_b(adapter, 1 if wraps else sweep)
                if sweep == 0 and wraps:
                    for g in range(GROUPS):
                        sp.wait_ge(group_used, turn(t, g) + 1)
                        for k in range(g * GC, (g + 1) * GC):
                            load_w(k, 1)
                if not (sweep == 1 and last):
                    sp.wait_ge(group_used, turn(t, GROUPS - 1) + 1)
                    load_x(j, j if last else seq + 2)
                sp.wait_ge(acc_read, t + 1)
                store(seq, j, sweep)
                if not (sweep == 1 and last):
                    sp.wait_ge(stored[j], DMA * (n + 1))
                    load_res(j if last else seq + 2, j, 1 if last else sweep)

            for sweep in range(SWEEPS):
                with sp.Fori(1 - sweep, PAIRS - 1) as i:
                    for j in range(2):
                        step(i, j, sweep, False)
                for j in range(2):
                    step(PAIRS - 1, j, sweep, True)
            for j in range(2):
                sp.wait_ge(stored[j], DMA * SWEEPS * PAIRS)

        @block.scalar
        def _(act):
            def x_high(g, t, j, n):
                if isinstance(t, int) and t < 2:
                    act.wait_ge(x_first[j][g], DMA)
                elif g == 0:
                    act.wait_ge(x_in[j], DMA * (n + GROUPS - 1))
                if not (isinstance(t, int) and turn(t, g) < GROUPS):
                    act.wait_ge(group_used, turn(t, g) - GROUPS + 1)
                s = slice(g * GC, (g + 1) * GC)
                nc.scalar.activation(x_hi[:, slot(t, g)], x_raw[:, j, s], COPY).then_inc(x_hi_done, 1)

            def w_high(k, sweep):
                act.wait_ge(w_in[k], DMA * (sweep + 1))
                nc.scalar.activation(w_hi[:, k, W_AT:W_AT + HALF], w_raw[:, k], COPY).then_inc(w_hi_done, 1)

            def a_high(t, j):
                act.wait_ge(a_in, DMA * (t + 1))
                if not (isinstance(t, int) and t < 2):
                    act.wait_ge(h_done, t - 1)
                nc.scalar.activation(w_hi[:, :, A_AT[j]:A_AT[j] + RANK], a_raw[:], COPY).then_inc(a_hi_done, 1)

            def b_high(t, j):
                act.wait_ge(b_in, DMA * (t + 1))
                if not (isinstance(t, int) and t < 2):
                    act.wait_ge(acc_done, t - 1)
                nc.scalar.activation(b_stack[0:P // 2, j], b_raw[:], COPY).then_inc(b_hi_done, 1)

            def h_high(t, j):
                act.wait_ge(h_done, t + 1)
                h = acc[j][:, H_BANK[j]:H_BANK[j] + 1, H_AT[j]:H_AT[j] + AC]
                nc.scalar.activation(h_cols[:, j, :, 0], h.to_broadcast([P, 2, AC]), COPY).then_inc(h_hi_done, 1)

            def h_out(t, j):
                act.wait_ge(h_turned, t + 1)
                if not (isinstance(t, int) and t < 2):
                    act.wait_ge(acc_done, t - 1)
                    act.wait_ge(h_kept, t - 1)
                nc.scalar.activation(h_stack[:, j], turned[:, 0:ROWS], COPY).then_inc(h_ready, 1)

            def step(i, j, sweep, last):
                t = sweep * SEQS + 2 * i + j
                jn, nn = 1 - j, sweep * PAIRS + i + j
                more = not (sweep == 1 and last and j == 1)
                wraps = sweep == 0 and last and j == 1
                if more:
                    x_high(0, t + 1, jn, nn)
                    if sweep == 0 and not wraps:
                        a_high(t + 1, jn)
                    b_high(t + 1, jn)
                    x_high(1, t + 1, jn, nn)
                if wraps:
                    for k in range(GC):
                        w_high(k, 1)
                if sweep == 0:
                    h_high(t, j)
                    h_out(t, j)
                if more:
                    x_high(2, t + 1, jn, nn)
                    x_high(3, t + 1, jn, nn)

            x_high(0, 0, 0, 0)
            a_high(0, 0)
            w_high(0, 0)
            x_high(0, 1, 1, 0)
            for k in range(1, GC):
                w_high(k, 0)
            a_high(1, 1)
            b_high(0, 0)
            for g in range(1, GROUPS):
                x_high(g, 0, 0, 0)
                x_high(g, 1, 1, 0)
                for k in range(g * GC, (g + 1) * GC):
                    w_high(k, 0)
            b_high(1, 1)
            h_high(0, 0)
            h_high(1, 1)
            h_out(0, 0)
            x_high(0, 2, 0, 1)
            h_out(1, 1)
            a_high(2, 0)
            b_high(2, 0)
            for g in range(1, GROUPS):
                x_high(g, 2, 0, 1)
            with act.Fori(1, PAIRS - 1) as i:
                for j in range(2):
                    step(i, j, 0, False)
            for j in range(2):
                step(PAIRS - 1, j, 0, True)
            for k in range(GC, CHUNKS):
                w_high(k, 1)
            with act.Fori(0, PAIRS - 1) as i:
                for j in range(2):
                    step(i, j, 1, False)
            for j in range(2):
                step(PAIRS - 1, j, 1, True)

        @block.vector
        def _(dve):
            def x_low(g, t, j):
                dve.wait_ge(x_hi_done, turn(t, g) + 1)
                s = slice(g * GC, (g + 1) * GC)
                nc.vector.tensor_tensor(x_lo[:, j, s], x_raw[:, j, s], x_hi[:, slot(t, g)],
                                        ALU.subtract).then_inc(x_split, 1)

            def w_low(k, sweep):
                dve.wait_ge(w_hi_done, sweep * CHUNKS + k + 1)
                nc.vector.tensor_tensor(w_lo[:, k], w_raw[:, k], w_hi[:, k, W_AT:W_AT + HALF],
                                        ALU.subtract).then_inc(w_split, 1)

            def a_low(t, j):
                dve.wait_ge(a_hi_done, t + 1)
                nc.vector.tensor_tensor(w_hi[:, :, A_AT[j] + RANK:A_AT[j] + AC], a_raw[:],
                                        w_hi[:, :, A_AT[j]:A_AT[j] + RANK], ALU.subtract).then_inc(a_ready, 1)

            def b_low(t, j):
                dve.wait_ge(b_hi_done, t + 1)
                nc.vector.tensor_tensor(b_stack[P // 2:P, j], b_raw[:], b_stack[0:P // 2, j],
                                        ALU.subtract).then_inc(b_ready, 1)

            def h_low(t, j):
                dve.wait_ge(h_hi_done, t + 1)
                h = acc[j][:, H_BANK[j]:H_BANK[j] + 1, H_AT[j]:H_AT[j] + AC]
                nc.vector.tensor_tensor(h_cols[:, j, :, 1], h.to_broadcast([P, 2, AC]), h_cols[:, j, :, 0],
                                        ALU.subtract).then_inc(h_cols_ready, 1)

            def finish(t, j, sweep):
                dve.wait_ge(res_biased, t + 1)
                dve.wait_ge(acc_done, t + 1)
                for o, low, n, first in pieces(sweep, j):
                    rows = res[:, j, first:first + n]
                    last = nc.vector.tensor_tensor(rows, acc[j][:, o, low:low + n], rows, ALU.add)
                last.then_inc(acc_read, 1)

            def step(i, j, sweep, last):
                t = sweep * SEQS + 2 * i + j
                more = not (sweep == 1 and last and j == 1)
                wraps = sweep == 0 and last and j == 1
                if more:
                    x_low(0, t + 1, 1 - j)
                    if sweep == 0 and not wraps:
                        a_low(t + 1, 1 - j)
                    b_low(t + 1, 1 - j)
                    x_low(1, t + 1, 1 - j)
                if wraps:
                    for k in range(GC):
                        w_low(k, 1)
                if sweep == 0:
                    h_low(t, j)
                finish(t, j, sweep)
                if more:
                    x_low(2, t + 1, 1 - j)
                    x_low(3, t + 1, 1 - j)

            x_low(0, 0, 0)
            a_low(0, 0)
            w_low(0, 0)
            x_low(0, 1, 1)
            for k in range(1, GC):
                w_low(k, 0)
            a_low(1, 1)
            b_low(0, 0)
            for g in range(1, GROUPS):
                x_low(g, 0, 0)
                x_low(g, 1, 1)
                for k in range(g * GC, (g + 1) * GC):
                    w_low(k, 0)
            b_low(1, 1)
            h_low(0, 0)
            h_low(1, 1)
            x_low(0, 2, 0)
            finish(0, 0, 0)
            a_low(2, 0)
            b_low(2, 0)
            finish(1, 1, 0)
            for g in range(1, GROUPS):
                x_low(g, 2, 0)
            with dve.Fori(1, PAIRS - 1) as i:
                for j in range(2):
                    step(i, j, 0, False)
            for j in range(2):
                step(PAIRS - 1, j, 0, True)
            for k in range(GC, CHUNKS):
                w_low(k, 1)
            with dve.Fori(0, PAIRS - 1) as i:
                for j in range(2):
                    step(i, j, 1, False)
            for j in range(2):
                step(PAIRS - 1, j, 1, True)

        @block.gpsimd
        def _(pool):
            nc.gpsimd.memset(eye_raw[:], 0.0).then_inc(eye_filled, 1)
            pool.wait_ge(eye_filled, 1)
            nc.gpsimd.affine_select(out=eye_raw[:], in_=eye_raw[:], compare_op=ALU.not_equal, fill=1.0, base=0,
                                    pattern=[[-1, P]], channel_multiplier=1).then_inc(eye_filled, 1)
            pool.wait_ge(eye_filled, 2)
            nc.gpsimd.tensor_copy(eye[:], eye_raw[:]).then_inc(eye_ready, 1)
            pool.wait_ge(bias_in, DMA)

            def step(i, j, sweep):
                seq = 2 * i + j
                t = sweep * SEQS + seq
                n = sweep * PAIRS + i
                if sweep == 1:
                    pool.wait_ge(acc_done, t - 1)
                    nc.gpsimd.tensor_copy(h_stack[:, j], h_keep[:, bass.ds(seq * ROWS, ROWS)]).then_inc(h_back, 1)
                pool.wait_ge(res_in[j], DMA * (n + 1))
                s = slice(sweep * HALF, (sweep + 1) * HALF)
                nc.gpsimd.tensor_tensor(res[:, j], res[:, j], bias_sb[:, s], ALU.add).then_inc(res_biased, 1)
                if sweep == 0:
                    pool.wait_ge(h_ready, t + 1)
                    nc.gpsimd.tensor_copy(h_keep[:, bass.ds(seq * ROWS, ROWS)], h_stack[:, j]).then_inc(h_kept, 1)

            with pool.Fori(0, PAIRS) as i:
                for j in range(2):
                    step(i, j, 0)
            pool.wait_ge(h_kept, SEQS)
            with pool.Fori(0, PAIRS) as i:
                for j in range(2):
                    step(i, j, 1)

        @block.tensor
        def _(pe):
            def with_a(t, g, k, j, part):
                xs = (x_hi[:, slot(t, g), k - g * GC], x_lo[:, j, k])[part]
                base = (0, W_AT)[j]
                for o in range(BANKS_A):
                    mm = nc.tensor.matmul(acc[j][:, o, 0:COLS_A], xs,
                                          w_hi[:, k, base + o * COLS_A:base + (o + 1) * COLS_A],
                                          start=(k == 0 and part == 0),
                                          stop=(k == CHUNKS - 1 and part == 1 and o == H_BANK[j]))
                return mm

            def with_w_lo(t, g, k, j, banks, after_h=False):
                for o, low, n, first in pieces(0, j):
                    if o in banks:
                        mm = nc.tensor.matmul(acc[j][:, o, low:low + n], x_hi[:, slot(t, g), k - g * GC],
                                              w_lo[:, k, first:first + n], start=False, stop=False,
                                              skip_group_check=after_h)
                return mm

            ALL = range(BANKS_A)

            def whole_group(t, g, j, w_waits=False):
                pe.wait_ge(x_split, turn(t, g) + 1)
                for k in range(g * GC, (g + 1) * GC):
                    if w_waits:
                        pe.wait_ge(w_hi_done, k + 1)
                    with_a(t, g, k, j, 0)
                    with_a(t, g, k, j, 1)
                    if w_waits:
                        pe.wait_ge(w_split, k + 1)
                    mm = with_w_lo(t, g, k, j, ALL)
                mm.then_inc(group_used, 1)

            def high_group(t, g, j, w_waits=False):
                pe.wait_ge(x_split, turn(t, g) + 1)
                for k in range(g * GC, (g + 1) * GC):
                    if w_waits:
                        pe.wait_ge(w_hi_done, k + 1)
                    with_a(t, g, k, j, 0)
                    mm = with_a(t, g, k, j, 1)
                if g == GROUPS - 1:
                    mm.then_inc(h_done, 1)

            def close(t, j, late):
                for g in late:
                    for k in range(g * GC, (g + 1) * GC):
                        with_w_lo(t, g, k, j, [o for o in ALL if o != H_BANK[j]])
                pe.wait_ge(h_cols_ready, t + 1)
                nc.tensor.matmul(turned[:, 0:ROWS], h_cols[:, j], eye[:], start=True, stop=True).then_inc(h_turned, 1)
                for g in late:
                    for k in range(g * GC, (g + 1) * GC):
                        mm = with_w_lo(t, g, k, j, [H_BANK[j]], after_h=True)
                    mm.then_inc(group_used, 1)
                pe.wait_ge(b_ready, t + 1)
                pe.wait_ge(h_ready, t + 1)
                low_rank(0, j)

            def low_rank(sweep, j):
                for o, low, n, first in pieces(sweep, j):
                    mm = nc.tensor.matmul(acc[j][:, o, low:low + n], h_stack[:, j], b_stack[:, j, first:first + n],
                                          start=False, stop=True,
                                          skip_group_check=(sweep == 0 and o == H_BANK[j]))
                mm.then_inc(acc_done, 1)

            for g in range(GROUPS - 1):
                for j in range(2):
                    if g == 0:
                        pe.wait_ge(a_ready, j + 1)
                    whole_group(j, g, j, w_waits=True)
            for j in range(2):
                high_group(j, GROUPS - 1, j, w_waits=True)
            pe.wait_ge(w_split, CHUNKS)
            pe.wait_ge(eye_ready, 1)
            for j in range(2):
                close(j, j, [GROUPS - 1])

            with pe.Fori(1, PAIRS) as i:
                for j in range(2):
                    t = 2 * i + j
                    pe.wait_ge(acc_read, t - 1)
                    pe.wait_ge(a_ready, t + 1)
                    for g in (0, 1):
                        whole_group(t, g, j)
                    for g in (2, 3):
                        high_group(t, g, j)
                    close(t, j, (2, 3))

            with pe.Fori(0, PAIRS) as i:
                for j in range(2):
                    t = SEQS + 2 * i + j
                    pe.wait_ge(acc_read, t - 1)
                    for g in range(GROUPS):
                        pe.wait_ge(x_split, turn(t, g) + 1)
                        for k in range(g * GC, (g + 1) * GC):
                            pe.wait_ge(w_split, CHUNKS + k + 1)
                            xh, xl = x_hi[:, g, k - g * GC], x_lo[:, j, k]
                            for n, (xs, ws, at0) in enumerate(((xh, w_hi, W_AT), (xl, w_hi, W_AT), (xh, w_lo, 0))):
                                for o in range(BANKS_W):
                                    mm = nc.tensor.matmul(acc[j][:, o], xs,
                                                          ws[:, k, at0 + o * BANK:at0 + (o + 1) * BANK],
                                                          start=(k == 0 and n == 0), stop=False)
                        mm.then_inc(group_used, 1)
                    pe.wait_ge(b_ready, t + 1)
                    pe.wait_ge(h_back, t - SEQS + 1)
                    low_rank(1, j)


def kernel(x, itok_B_6_15, L0_cond_base_weight, L0_cond_base_bias, L0_cond_lora_A_w, L0_cond_lora_B_w):
    import concourse.bacc as bacc
    from concourse.bass_utils import run_bass_kernel_spmd

    def laid(a):
        return np.ascontiguousarray(a)

    x = np.asarray(x)
    w = np.asarray(L0_cond_base_weight)
    a = np.asarray(L0_cond_lora_A_w)
    b = np.asarray(L0_cond_lora_B_w)
    arrays = {
        "xT": laid(x.reshape(SEQS, ROWS, CHUNKS, P).transpose(0, 3, 2, 1)),
        "x": laid(x),
        "wT": laid(w.reshape(SWEEPS, HALF, CHUNKS, P).transpose(0, 2, 3, 1)),
        "bias": laid(np.asarray(L0_cond_base_bias).reshape(1, D_OUT)),
        "aT": laid(a.reshape(ADAPTERS, RANK, CHUNKS, P).transpose(0, 3, 2, 1)),
        "bT": laid(b.transpose(0, 2, 1)),
        "ids": laid(np.asarray(itok_B_6_15).reshape(1, SEQS)),
    }
    nc = bacc.Bacc("TRN2", target_bir_lowering=False, num_devices=1)
    aps = [nc.dram_tensor(name, v.shape, mybir.dt.from_np(v.dtype), kind="ExternalInput").ap()
           for name, v in arrays.items()]
    out = nc.dram_tensor("out", (SEQS, ROWS, D_OUT), mybir.dt.float32, kind="ExternalOutput").ap()
    lora_kernel(nc, *aps, out)
    r = run_bass_kernel_spmd(nc, [arrays], core_ids=[0])
    return r.results[0]["out"]
```
